# Optimizing a Trainium2 kernel written in Bass

```python
import numpy as np
import jax
import jax.numpy as jnp

def _softmax(x, axis=-1):
    return jax.nn.softmax(x, axis=axis)

def _gelu(x):
    return jax.nn.gelu(x, approximate=True)

def _silu(x):
    return jax.nn.silu(x)

def _sigmoid(x):
    return jax.nn.sigmoid(x)

def _layernorm(x, axis=-1, eps=1e-05):
    m = jnp.mean(x, axis=axis, keepdims=True)
    v = jnp.var(x, axis=axis, keepdims=True)
    return (x - m) / jnp.sqrt(v + eps)

def _scatter_add(tgt, idx, src, axis=0):
    return tgt.at[idx].add(src)

def _segment_sum(src, seg, n):
    return jax.ops.segment_sum(src, seg, n)
kernel_name = 'mk_adj_preln_d1_adj_r2_1dba7e'

def setup_inputs(seed: int=0):
    np.random.seed(seed)
    _w = jnp.asarray

    def _rec_inputs():
        import jax
        import jax.numpy as jnp
        _gk = jax.random.key(seed)
        x = -0.0002928 + 1 * jax.random.normal(jax.random.fold_in(_gk, 1), (4096, 256), jnp.float32)
        _a = jax.random.bernoulli(jax.random.fold_in(_gk, 2), 0.000488281, (4096, 4096))
        _a = jnp.logical_or(_a, jnp.swapaxes(_a, -1, -2))
        _a = jnp.logical_or(_a, jnp.eye(4096, dtype=bool))
        _af = _a.astype(jnp.float32)
        _af = _af * jax.random.uniform(jax.random.fold_in(_gk, 3), (4096, 4096), jnp.float32, 0.05, 1)
        adj = _af
        return (x, adj)
    x, adj = _rec_inputs()

    def _L0_gnn_setup():
        import jax, jax.numpy as jnp
        import numpy as np
        N = 4096
        DIN = 256
        DOUT = 256
        key = jax.random.key(seed)
        k1, k2, k3 = jax.random.split(key, 3)
        x = jax.random.normal(k1, (N, DIN), dtype=jnp.float32)
        adj = jax.random.uniform(k2, (N, N), dtype=jnp.float32)
        W = jax.random.normal(k3, (DIN, DOUT), dtype=jnp.float32) * (1.0 / np.sqrt(DIN))
        b = jnp.zeros((DOUT,), dtype=jnp.float32)
        return {'x': x, 'adj': adj, 'W': W, 'b': b}
    _L0_gnn_all = _L0_gnn_setup()
    _L0_gnn_in = {k: v for k, v in _L0_gnn_all.items() if k in ('W', 'b')}
    del _L0_gnn_all
    return {'x': x, 'adj': adj, 'L0_gnn_W': _L0_gnn_in['W'], 'L0_gnn_b': _L0_gnn_in['b']}

def reference(x, adj, L0_gnn_W, L0_gnn_b):
    import jax
    import jax.numpy as jnp

    def _L0_gnn_ref(x, adj, W, b):
        import jax, jax.numpy as jnp
        import numpy as np
        N = 4096
        DIN = 256
        DOUT = 256
        rowsum = adj.sum(axis=1)
        d_inv_sqrt = jnp.where(rowsum > 0, rowsum ** (-0.5), 0.0)
        normalized_adj = d_inv_sqrt[:, None] * adj * d_inv_sqrt[None, :]
        support = normalized_adj @ x
        out = support @ W + b
        return jax.nn.relu(out)
    h = jnp.maximum(_layernorm(x, axis=-1), 0.0)
    x = x + _L0_gnn_ref(h, adj, L0_gnn_W, L0_gnn_b)
    return x

_drawn_inputs = setup_inputs


def setup_inputs(seed=0):
    import zlib

    import numpy as np

    out = dict(_drawn_inputs(seed))
    spreads = {'L0_gnn_b': (0.0, 0.1)}
    factors = {}
    for name, (base, spread) in spreads.items():
        noise = np.random.default_rng([zlib.crc32(name.encode()), seed]).standard_normal(out[name].shape)
        drawn = base * np.exp(spread * noise) if base else spread * noise
        out[name] = jnp.asarray(drawn.astype(out[name].dtype))
    for name, factor in factors.items():
        out[name] = (out[name] * factor).astype(out[name].dtype)
    return out
```

```python
from contextlib import ExitStack

import numpy as np

import concourse.bass as bass
from concourse import mybir

ALU = mybir.AluOpType
ACT = mybir.ActivationFunctionType
F32 = mybir.dt.float32
BF16 = mybir.dt.bfloat16

P = 128
QN = 4
R = 32
BANK = 512
DMA = 16
EPS = 1e-5
TINY = float(np.finfo(np.float32).tiny)


def at_least(eng, sem, value):
    if not isinstance(value, int) or value > 0:
        eng.wait_ge(sem, value)


def build(nc, x, adj, w, b, out):
    N, D = x.shape
    SPAN = N // QN
    NT = SPAN // R
    TG = 4
    NS = NT // TG
    GW = TG * R
    KD = D // P
    XP = 4
    XT = NT // XP

    adj_rows = adj.rearrange("(q t r) c -> t r q c", q=QN, r=R)
    x_rows = x.rearrange("(q t r) f -> q r t f", q=QN, r=R)
    out_rows = out.rearrange("(q t r) f -> t q r f", q=QN, r=R)

    def left_groups(T):
        return TG * (T * (T - 1) // 2 + T)

    def right_groups(T):
        return left_groups(NS) + TG * sum(NS - 1 - u for u in range(T))

    with ExitStack() as ctx:
        def sb(name, shape, dt=F32):
            return ctx.enter_context(nc.sbuf_tensor(name, shape, dt))

        def ps(name, shape):
            return ctx.enter_context(nc.psum_tensor(name, shape, F32))

        def sem(name):
            return ctx.enter_context(nc.semaphore(name))

        x_sb = sb("x_sb", [P, NT, D])
        w_sb = sb("w_sb", [P, KD, D])
        b_sb = sb("b_sb", [P, D])
        ident = sb("ident", [P, P])
        same_r = sb("same_r", [P, P])
        own_q = sb("own_q", [P, QN])
        minus_half = sb("minus_half", [P, XT])
        stats = sb("stats", [P, NT, 6])
        mean2 = sb("mean2", [P, XT])
        mean_dif = sb("mean_dif", [P, XT])
        mean_dif2 = sb("mean_dif2", [P, XT])
        m2 = sb("m2", [P, XT])
        m2_eps = sb("m2_eps", [P, XT])
        mean = sb("mean", [P, NT])
        var = sb("var", [P, NT])
        rstd = sb("rstd", [P, NT])
        xn = [sb(f"xn{e}", [P, D]) for e in range(2)]
        hT = [sb(f"hT{e}", [P, D]) for e in range(2)]
        natural = [sb(f"natural{e}", [P, QN, SPAN]) for e in range(2)]
        diag = [sb(f"diag{u}", [P, TG, QN, GW]) for u in range(2)]
        at = [sb(f"at{k}", [P, TG, P]) for k in range(2)]
        junk = sb("junk", [P, QN, SPAN], BF16)
        part_sum = sb("part_sum", [P, NT, QN])
        own_part = sb("own_part", [P, QN])
        row_sum = sb("row_sum", [P, 1])
        row_safe = [sb(f"row_safe{e}", [P, 1]) for e in range(2)]
        row_pos = [sb(f"row_pos{e}", [P, 1]) for e in range(2)]
        row_pow = sb("row_pow", [P, 1])
        d = sb("d", [P, NT])
        G = sb("G", [P, NT, D])
        acc = sb("acc", [P, NT - TG, D])
        total = sb("total", [P, D])
        biased = sb("biased", [P, D])
        result = [sb(f"result{e}", [P, D]) for e in range(2)]

        bank = ps("bank", [P, TG, BANK])
        ps_hT = [ps(f"ps_hT{e}", [P, BANK]) for e in range(2)]
        ps_sum = [ps(f"ps_sum{e}", [P, BANK]) for e in range(2)]

        x_landed = [sem(f"x_landed{c}") for c in range(XP)]
        w_landed = sem("w_landed")
        b_landed = sem("b_landed")
        consts_made = sem("consts_made")
        stats_step = sem("stats_step")
        var_ready = sem("var_ready")
        rstd_ready = sem("rstd_ready")
        xn_ready = sem("xn_ready")
        hT_made = sem("hT_made")
        hT_ready = sem("hT_ready")
        hw_made = sem("hw_made")
        hw_ready = sem("hw_ready")
        natural_landed = [sem(f"natural_landed{e}") for e in range(2)]
        natural_summed = sem("natural_summed")
        diag_copied = sem("diag_copied")
        sum_made = sem("sum_made")
        own_summed = sem("own_summed")
        sum_ready = sem("sum_ready")
        pow_done = sem("pow_done")
        d_ready = sem("d_ready")
        G_ready = sem("G_ready")
        at_ready = sem("at_ready")
        at_used = sem("at_used")
        acc_saved = sem("acc_saved")
        bank_taken = sem("bank_taken")
        biased_ready = sem("biased_ready")
        result_ready = sem("result_ready")
        stored = [sem(f"stored{e}") for e in range(2)]
        pool_step = sem("pool_step")

        block = ctx.enter_context(nc.Block())

        def pairs(eng, T):
            if T == 0:
                yield from range(2)
            else:
                with eng.Fori(0, 2) as h:
                    yield h

        def row(T, h, e):
            return TG * T + 2 * h + e

        @block.sync
        def _(sp):
            for c in range(XP):
                for q in range(QN):
                    sp.dma_start(x_sb[q * R:(q + 1) * R, c * XT:(c + 1) * XT, :],
                                 x_rows[q, :, c * XT:(c + 1) * XT, :]).then_inc(x_landed[c], DMA)
                if c == 0:
                    sp.dma_start(w_sb[:, :, :], w.rearrange("(k p) n -> p k n", p=P)).then_inc(w_landed, DMA)
                    sp.dma_start(b_sb[:, :], b.partition_broadcast(P)).then_inc(b_landed, DMA)

            def load(e, t, first):
                for q in range(QN):
                    sp.dma_start(natural[e][q * R:(q + 1) * R, :, first:SPAN],
                                 adj_rows[t, :, :, q * SPAN + first:(q + 1) * SPAN]).then_inc(
                                     natural_landed[e], DMA)

            for T in range(NS):
                for h in pairs(sp, T // 2):
                    for e in range(2):
                        n = row(T, h, e)
                        if T >= 1:
                            before = left_groups(T - 1) + (3 + e) * (T - 1)
                            within = left_groups(T) + (1 + e) * T
                            at_least(sp, at_ready, h * (within - before) + before)
                        at_least(sp, natural_summed, n - 1)
                        at_least(sp, diag_copied, n - 1)
                        load(e, n, 0)
            for T in range(NS - 1):
                for h in pairs(sp, 1):
                    for e in range(2):
                        if T == 0:
                            before = left_groups(NS - 1) + (3 + e) * (NS - 1)
                            sp.wait_ge(natural_summed, NT)
                            sp.wait_ge(diag_copied, NT)
                        else:
                            before = right_groups(T - 1) + (3 + e) * (NS - T)
                        within = right_groups(T) + (1 + e) * (NS - 1 - T)
                        sp.wait_ge(at_ready, h * (within - before) + before)
                        load(e, row(T, h, e), GW * (T + 1))

        @block.scalar
        def _(act):
            for T in range(NS):
                for h in pairs(act, T):
                    for e in range(2):
                        n = row(T, h, e)
                        act.wait_ge(natural_landed[e], QN * DMA * (2 * T + h + 1))
                        at_least(act, natural_summed, n)
                        for q in range(QN):
                            last = nc.scalar.activation(junk[:, q, :], natural[e][:, q, :], ACT.Copy,
                                                        accum_out=part_sum[:, n, q:q + 1])
                        last.then_inc(natural_summed, 1)
                        if T >= 1:
                            act.wait_ge(at_used, left_groups(T) - TG + 2 * h + e + 1)
                            nc.scalar.copy(acc[:, n - TG, :], bank[:, 2 * h + e, 0:D]).then_inc(acc_saved, 1)

            def store(e, k, t):
                act.wait_ge(result_ready, k + 1)
                for q in range(QN):
                    act.dma_start(out_rows[t, q], result[e][q * R:(q + 1) * R, :]).then_inc(stored[e], DMA)

            for s in range(TG):
                store(s % 2, s, NT - TG + s)
            with act.Fori(0, (NT - TG) // 2) as i:
                for e in range(2):
                    store(e, TG + 2 * i + e, 2 * i + e)
            for e in range(2):
                act.wait_ge(stored[e], QN * DMA * (NT // 2))

        @block.gpsimd
        def _(pool):
            step = [0]

            def then(ins):
                step[0] += 1
                ins.then_inc(pool_step, 1)
                pool.wait_ge(pool_step, step[0])

            then(nc.gpsimd.memset(minus_half[:, :], -0.5))
            then(nc.gpsimd.memset(ident[:, :], 0.0))
            then(nc.gpsimd.memset(same_r[:, :], 0.0))
            then(nc.gpsimd.memset(own_q[:, :], 0.0))
            then(nc.gpsimd.affine_select(out=ident[:, :], in_=ident[:, :], compare_op=ALU.not_equal, fill=1.0,
                                         base=0, pattern=[[-1, P]], channel_multiplier=1))
            for q in range(QN):
                v = same_r[:, :].rearrange("p (a r) -> p a r", a=QN)
                then(nc.gpsimd.affine_select(out=v, in_=v, compare_op=ALU.not_equal, fill=1.0,
                                             base=-q * R, pattern=[[0, QN], [-1, R]], channel_multiplier=1))
                then(nc.gpsimd.memset(own_q[q * R:(q + 1) * R, q:q + 1], 1.0))
            pool.sem_inc(consts_made, 1)

            for c in range(XP):
                pool.wait_ge(var_ready, c + 1)
                nc.gpsimd.tensor_tensor(out=rstd[:, c * XT:(c + 1) * XT], in0=var[:, c * XT:(c + 1) * XT],
                                        in1=minus_half[:, :], op=ALU.pow).then_inc(rstd_ready, 1)

            for T in range(NS):
                for h in pairs(pool, T):
                    for e in range(2):
                        n = row(T, h, e)
                        pool.wait_ge(natural_landed[e], QN * DMA * (2 * T + h + 1))
                        if T >= 2:
                            pool.wait_ge(at_ready, left_groups(T - 1))
                        nc.gpsimd.tensor_copy(diag[T % 2][:, 2 * h + e],
                                              natural[e][:, :, T * GW:(T + 1) * GW]).then_inc(diag_copied, 1)
                        pool.wait_ge(sum_ready, n + 1)
                        nc.gpsimd.tensor_tensor(out=row_pow[:, :], in0=row_safe[e][:, :],
                                                in1=minus_half[:, 0:1], op=ALU.pow).then_inc(pow_done, 1)
                        pool.wait_ge(pow_done, n + 1)
                        nc.gpsimd.tensor_tensor(out=d[:, bass.ds(n, 1)], in0=row_pow[:, :],
                                                in1=row_pos[e][:, :], op=ALU.mult).then_inc(d_ready, 1)

        @block.vector
        def _(dve):
            stats_k = 0
            for c in range(XP):
                tiles = slice(c * XT, (c + 1) * XT)
                dve.wait_ge(x_landed[c], QN * DMA)
                with dve.Fori(c * XT, (c + 1) * XT) as t:
                    nc.vector.bn_stats(stats[:, t, :], x_sb[:, t, :]).then_inc(stats_step, 1)
                stats_k += XT
                dve.wait_ge(stats_step, stats_k)
                st = stats[:, tiles, :]
                nc.vector.tensor_tensor(out=mean2[:, :], in0=st[:, :, 1], in1=st[:, :, 4], op=ALU.add)
                nc.vector.tensor_tensor(out=mean_dif[:, :], in0=st[:, :, 1], in1=st[:, :, 4], op=ALU.subtract)
                nc.vector.tensor_tensor(out=m2[:, :], in0=st[:, :, 2], in1=st[:, :, 5],
                                        op=ALU.add).then_inc(stats_step, 1)
                stats_k += 1
                dve.wait_ge(stats_step, stats_k)
                nc.vector.tensor_scalar(mean[:, tiles], mean2[:, :], 0.5, None, ALU.mult)
                nc.vector.tensor_tensor(out=mean_dif2[:, :], in0=mean_dif[:, :], in1=mean_dif[:, :], op=ALU.mult)
                nc.vector.tensor_scalar(m2_eps[:, :], m2[:, :], 1.0 / D, EPS, ALU.mult,
                                        ALU.add).then_inc(stats_step, 1)
                stats_k += 1
                dve.wait_ge(stats_step, stats_k)
                nc.vector.scalar_tensor_tensor(out=var[:, tiles], in0=mean_dif2[:, :], scalar=0.25,
                                               in1=m2_eps[:, :], op0=ALU.mult, op1=ALU.add).then_inc(var_ready, 1)

            def normalise(i):
                for e in range(2):
                    t = 2 * i + e
                    at_least(dve, hT_made, t - 1)
                    nc.vector.tensor_scalar(xn[e][:, :], x_sb[:, t, :], mean[:, bass.ds(t, 1)],
                                            rstd[:, bass.ds(t, 1)], ALU.subtract, ALU.mult).then_inc(xn_ready, 1)

            def rectify(i):
                for e in range(2):
                    t = 2 * i + e
                    dve.wait_ge(hT_made, t + 1)
                    at_least(dve, hw_made, t - 1)
                    nc.vector.tensor_scalar(hT[e][:, :], ps_hT[e][:, 0:D], 0.0, None,
                                            ALU.max).then_inc(hT_ready, 1)

            def take_hw(i):
                for e in range(2):
                    t = 2 * i + e
                    dve.wait_ge(hw_made, t + 1)
                    nc.vector.tensor_copy(G[:, t, :], bank[:, e, 0:D]).then_inc(hw_ready, 1)

            dve.wait_ge(rstd_ready, XP)
            normalise(0)
            rectify(0)
            normalise(1)
            take_hw(0)
            with dve.Fori(1, NT // 2 - 1) as i:
                rectify(i)
                normalise(i + 1)
                take_hw(i)
            rectify(NT // 2 - 1)
            take_hw(NT // 2 - 1)

            def move(k, slot, src):
                at_least(dve, at_used, k - 1)
                nc.vector.transpose(at[slot][:, :, :].rearrange("p t (q r) -> p q t r", q=QN),
                                    src.rearrange("p q (t c) -> p q t c", c=R)).then_inc(at_ready, 1)

            def finish(e, k, t, used, summed):
                nc.vector.scalar_tensor_tensor(out=biased[:, :], in0=summed, scalar=d[:, bass.ds(t, 1)],
                                               in1=b_sb[:, :], op0=ALU.mult, op1=ALU.add).then_inc(biased_ready, 1)
                dve.wait_ge(biased_ready, k + 1)
                at_least(dve, stored[e], QN * DMA * used)
                nc.vector.scalar_tensor_tensor(out=result[e][:, :], in0=biased[:, :], scalar=0.0,
                                               in1=x_sb[:, t, :], op0=ALU.max, op1=ALU.add).then_inc(result_ready, 1)

            dve.wait_ge(consts_made, 1)
            dve.wait_ge(hw_ready, NT)
            for T in range(NS):
                for h in pairs(dve, T):
                    for e in range(2):
                        n = row(T, h, e)
                        dve.wait_ge(natural_landed[e], QN * DMA * (2 * T + h + 1))

                        def row_sums():
                            dve.wait_ge(sum_made, n + 1)
                            nc.vector.tensor_tensor_reduce(
                                out=own_part[:, :], in0=ps_sum[e][:, 0:QN], in1=own_q[:, :], scale=1.0,
                                scalar=0.0, op0=ALU.mult, op1=ALU.add,
                                accum_out=row_sum[:, :]).then_inc(own_summed, 1)
                            dve.wait_ge(own_summed, n + 1)
                            at_least(dve, d_ready, n - 1)
                            nc.vector.tensor_scalar(row_safe[e][:, :], row_sum[:, :], TINY, None, ALU.max)
                            nc.vector.tensor_scalar(row_pos[e][:, :], row_sum[:, :], 0.0, None,
                                                    ALU.is_gt).then_inc(sum_ready, 1)

                        if T == 0:
                            row_sums()
                        for g in range(T):
                            k = left_groups(T) + (2 * h + e) * T + g
                            move(k, (e * T + g) % 2, natural[e][:, :, g * GW:(g + 1) * GW])
                            if g == min(1, T - 1):
                                row_sums()
                        dve.wait_ge(d_ready, n + 1)
                        nc.vector.tensor_scalar(G[:, n, :], G[:, n, :], d[:, bass.ds(n, 1)], None,
                                                ALU.mult).then_inc(G_ready, 1)
                for s in range(TG):
                    if s == 0:
                        dve.wait_ge(diag_copied, TG * (T + 1))
                    move(left_groups(T) + TG * T + s, s % 2, diag[T % 2][:, s])
            for s in range(TG):
                dve.wait_ge(at_used, left_groups(NS) - TG + s + 1)
                nc.vector.tensor_copy(total[:, :], bank[:, s, 0:D]).then_inc(bank_taken, 1)
                dve.wait_ge(bank_taken, s + 1)
                finish(s % 2, s, NT - TG + s, s // 2, total[:, :])

            def finish_right(n, s, e, used, group_end):
                dve.wait_ge(at_used, group_end)
                nc.vector.tensor_tensor(out=total[:, :], in0=bank[:, s, 0:D], in1=acc[:, n, :],
                                        op=ALU.add).then_inc(bank_taken, 1)
                dve.wait_ge(bank_taken, TG + n + 1)
                finish(e, TG + n, n, used, total[:, :])

            dve.wait_ge(acc_saved, NT - TG)
            for T in range(NS - 1):
                W = NS - 1 - T
                for h in pairs(dve, T):
                    for e in range(2):
                        n = row(T, h, e)
                        dve.wait_ge(natural_landed[e], QN * DMA * (NT // 2 + 2 * T + h + 1))
                        for g in range(W):
                            k = right_groups(T) + (2 * h + e) * W + g
                            move(k, (e * W + g) % 2, natural[e][:, :, (T + 1 + g) * GW:(T + 2 + g) * GW])
                            if g == min(1, W - 1):
                                k_row = right_groups(T) + (2 * h + e) * W
                                if e == 1:
                                    finish_right(n - 1, 2 * h, 0, 2 + 2 * T + h, k_row)
                                elif T == 0 and h == 1:
                                    finish_right(n - 1, 1, 1, 2, k_row)
                                elif T > 0:
                                    finish_right(n - 1, h * -2 + 3, 1, 1 + 2 * T + h, k_row)
            n = NT - TG - 1
            finish_right(n, TG - 1, 1, 1 + NT // 2 - 2, right_groups(NS - 1))

        @block.tensor
        def _(pe):
            def transpose_rows(i):
                for e in range(2):
                    t = 2 * i + e
                    pe.wait_ge(xn_ready, t + 1)
                    at_least(pe, hT_ready, t - 1)
                    for f in range(KD):
                        last = nc.tensor.transpose(ps_hT[e][:, f * P:(f + 1) * P], xn[e][:, f * P:(f + 1) * P],
                                                   ident[:, :])
                    last.then_inc(hT_made, 1)

            def project(i):
                for e in range(2):
                    t = 2 * i + e
                    pe.wait_ge(hT_ready, t + 1)
                    at_least(pe, hw_ready, t - 1)
                    for f in range(KD):
                        last = nc.tensor.matmul(bank[:, e, 0:D], hT[e][:, f * P:(f + 1) * P], w_sb[:, f, :],
                                                start=(f == 0), stop=(f == KD - 1))
                    last.then_inc(hw_made, 1)

            pe.wait_ge(consts_made, 1)
            pe.wait_ge(w_landed, DMA)
            transpose_rows(0)
            transpose_rows(1)
            project(0)
            with pe.Fori(1, NT // 2 - 1) as i:
                transpose_rows(i + 1)
                project(i)
            project(NT // 2 - 1)

            def multiply(k, slot, s, g, first, last):
                pe.wait_ge(at_ready, k + 1)
                for j in range(TG):
                    mm = nc.tensor.matmul(bank[:, s, 0:D], at[slot][:, j, :], G[:, g * TG + j, :],
                                          start=(first and j == 0), stop=(last and j == TG - 1))
                mm.then_inc(at_used, 1)

            pe.wait_ge(hw_ready, NT)
            for T in range(NS):
                for h in pairs(pe, T):
                    for e in range(2):
                        n = row(T, h, e)
                        pe.wait_ge(natural_summed, n + 1)
                        at_least(pe, own_summed, n - 1)
                        nc.tensor.matmul(ps_sum[e][:, 0:QN], same_r[:, :], part_sum[:, n, :],
                                         start=True, stop=True).then_inc(sum_made, 1)
                        if T >= 1:
                            pe.wait_ge(acc_saved, n - TG + 1)
                        for g in range(T):
                            k = left_groups(T) + (2 * h + e) * T + g
                            multiply(k, (e * T + g) % 2, 2 * h + e, g, g == 0, False)
                pe.wait_ge(G_ready, TG * (T + 1))
                for s in range(TG):
                    multiply(left_groups(T) + TG * T + s, s % 2, s, T, T == 0, True)
            for T in range(NS - 1):
                W = NS - 1 - T
                for h in pairs(pe, T):
                    for e in range(2):
                        n = row(T, h, e)
                        pe.wait_ge(bank_taken, n + 1)
                        for g in range(W):
                            k = right_groups(T) + (2 * h + e) * W + g
                            multiply(k, (e * W + g) % 2, 2 * h + e, T + 1 + g, g == 0, g == W - 1)


INPUTS = ["x", "adj", "L0_gnn_W", "L0_gnn_b"]


def kernel(**inputs):
    import concourse.bacc as bacc
    from concourse.bass_utils import run_bass_kernel_spmd

    nc = bacc.Bacc("TRN2", target_bir_lowering=False, num_devices=1)
    arrays, args = {}, []
    for name in INPUTS:
        a = np.ascontiguousarray(inputs[name])
        arrays[f"in_{name}"] = a
        args.append(nc.dram_tensor(f"in_{name}", a.shape, mybir.dt.from_np(a.dtype), kind="ExternalInput").ap())
    out = nc.dram_tensor("out", arrays["in_x"].shape, F32, kind="ExternalOutput").ap()
    build(nc, *args, out)
    r = run_bass_kernel_spmd(nc, [arrays], core_ids=[0])
    return r.results[0]["out"]
```

```python
from contextlib import ExitStack

import numpy as np

import concourse.bass as bass
from concourse import mybir

ALU = mybir.AluOpType
ACT = mybir.ActivationFunctionType
AX = mybir.AxisListType
F32 = mybir.dt.float32
BF16 = mybir.dt.bfloat16
F32R = mybir.dt.float32r

P = 128
QN = 4
R = 32
BANK = 512
DMA = 16
EPS = 1e-5
TINY = float(np.finfo(np.float32).tiny)


def at_least(eng, sem, value):
    if not isinstance(value, int) or value > 0:
        eng.wait_ge(sem, value)


def build(nc, x, adj, w, b, out):
    N, D = x.shape
    SPAN = N // QN
    NT = SPAN // R
    TG = 4
    NS = NT // TG
    GW = TG * R
    KD = D // P
    XP = 4
    XT = NT // XP
    AR = 4
    RING = 4
    SUMMED = 5
    FIRST_TAKES = 12
    QA = QN - 1
    SPLIT = 1
    BUSY = 4
    LAG = 2

    adj_rows = adj.rearrange("(q t r) c -> t r q c", q=QN, r=R)
    x_rows = x.rearrange("(q t r) f -> q r t f", q=QN, r=R)
    out_rows = out.rearrange("(q t r) f -> t q r f", q=QN, r=R)

    def left_groups(T):
        return TG * (T * (T - 1) // 2 + T)

    def left_end(n):
        T, s = divmod(n, TG)
        return left_groups(T) + (s + 1) * T

    def right_groups(T):
        return left_groups(NS) + TG * sum(NS - 1 - u for u in range(T + 1, NS - 1))

    def place(k):
        return (NS - 1 - k // TG) * TG + k % TG

    def group_end(k):
        W, s = divmod(k, TG)
        return left_groups(NS) - TG + s + 1 if W == 0 else right_groups(NS - 1 - W) + (s + 1) * W

    def finished(groups):
        return sum(group_end(k) + LAG <= groups for k in range(NT)) if groups > left_groups(NS) else 0

    loads = []
    for T in reversed(range(NS - 1)):
        rows = 4 if NS - 1 - T <= 2 else 2 if NS - 1 - T <= 4 else 1
        loads += [(T, s, rows) for s in range(0, TG, rows)]

    def load_end(u):
        T, s, rows = loads[u]
        return right_groups(T) + (s + rows) * (NS - 1 - T)

    with ExitStack() as ctx:
        def sb(name, shape, dt=F32):
            return ctx.enter_context(nc.sbuf_tensor(name, shape, dt))

        def ps(name, shape):
            return ctx.enter_context(nc.psum_tensor(name, shape, F32))

        def sem(name):
            return ctx.enter_context(nc.semaphore(name))

        w_sb = sb("w_sb", [P, KD, D])
        b_sb = sb("b_sb", [P, D])
        ident = sb("ident", [P, P])
        same_r = sb("same_r", [P, P])
        own_q = sb("own_q", [P, QN])
        minus_half = sb("minus_half", [P, XT])
        stats = sb("stats", [P, NT, 6])
        mean2 = sb("mean2", [P, XT])
        mean_dif = sb("mean_dif", [P, XT])
        mean_dif2 = sb("mean_dif2", [P, XT])
        m2 = sb("m2", [P, XT])
        m2_eps = sb("m2_eps", [P, XT])
        mean = sb("mean", [P, NT])
        var = sb("var", [P, NT])
        rstd = sb("rstd", [P, NT])
        natural = [sb(f"natural{s}", [P, QN, SPAN]) for s in range(TG)]
        diag = [sb(f"diag{s}", [P, QN, GW]) for s in range(TG)]
        at = [sb(f"at{k}", [P, TG, P]) for k in range(RING)]
        hi = [sb(f"hi{k}", [P, TG, P], F32R) for k in range(RING)]
        lo = [sb(f"lo{k}", [P, TG, P], F32R) for k in range(RING)]
        part_sum = sb("part_sum", [P, NT, QN])
        own_part = sb("own_part", [P, QN])
        row_sum = sb("row_sum", [P, 1])
        row_safe = [sb(f"row_safe{e}", [P, 1]) for e in range(2)]
        row_pos = [sb(f"row_pos{e}", [P, 1]) for e in range(2)]
        row_pow = sb("row_pow", [P, 1])
        d = sb("d", [P, NT])
        G = sb("G", [P, NT, 2, D], F32R)
        acc = sb("acc", [P, NT, D])
        x_again = sb("x_again", [P, TG, D])
        result = [sb(f"result{s}", [P, D]) for s in range(TG)]

        def half(k, i):
            return at[k][:, 2 * i:2 * i + 2, :].rearrange("p t r -> p (t r)")

        centred = [half(j // 2, j % 2) for j in range(AR)]
        hT = [half(2 + j // 2, j % 2) for j in range(AR)]
        hi_total, total = w_sb[:, 0, :], w_sb[:, 1, :]
        junk = [x_again[:, 2 * i:2 * i + 2, :].rearrange("p s f -> p (s f)").bitcast(BF16) for i in range(2)]

        bank = ps("bank", [P, TG, BANK])
        ps_hT = [ps(f"ps_hT{j}", [P, BANK]) for j in range(AR)]
        ps_sum = ps_hT[0:2]

        x_landed = [sem(f"x_landed{c}") for c in range(XP)]
        x_again_landed = [sem(f"x_again_landed{s}") for s in range(TG)]
        w_landed = sem("w_landed")
        b_landed = sem("b_landed")
        consts_made = sem("consts_made")
        stats_step = sem("stats_step")
        mean_ready = sem("mean_ready")
        var_ready = sem("var_ready")
        rstd_ready = sem("rstd_ready")
        centred_ready = sem("centred_ready")
        hT_made = sem("hT_made")
        hT_ready = sem("hT_ready")
        hw_made = sem("hw_made")
        hw_ready = sem("hw_ready")
        natural_landed = [sem(f"natural_landed{s}") for s in range(TG)]
        quarter_summed = sem("quarter_summed")
        last_summed = sem("last_summed")
        diag_copied = sem("diag_copied")
        sum_made = sem("sum_made")
        own_summed = sem("own_summed")
        sum_ready = sem("sum_ready")
        pow_done = sem("pow_done")
        d_ready = sem("d_ready")
        G_ready = sem("G_ready")
        at_ready = sem("at_ready")
        hi_ready = sem("hi_ready")
        lo_ready = sem("lo_ready")
        lo_ready2 = sem("lo_ready2")
        group_used = sem("group_used")
        G_hi_made = sem("G_hi_made")
        acc_saved = sem("acc_saved")
        hi_totalled = sem("hi_totalled")
        bank_taken = sem("bank_taken")
        biased_ready = sem("biased_ready")
        result_ready = sem("result_ready")
        stored = [sem(f"stored{s}") for s in range(TG)]
        pool_step = sem("pool_step")

        block = ctx.enter_context(nc.Block())

        def rows_of(eng, groups):
            if groups and 2 * groups % RING == 0:
                with eng.Fori(0, 2) as h:
                    for e in range(2):
                        yield 2 * h + e, e * groups
            else:
                for s in range(TG):
                    yield s, s * groups

        def right_part(slot, i, T):
            width = (NS - 1 - T) * GW
            flat = natural[slot][:, :, :].rearrange("p q c -> p (q c)")
            return flat[:, i * QN * width:(i + 1) * QN * width].rearrange("p (q c) -> p q c", q=QN)

        @block.sync
        def _(sp):
            for c in range(XP):
                for q in range(QN):
                    sp.dma_start(acc[q * R:(q + 1) * R, c * XT:(c + 1) * XT, :],
                                 x_rows[q, :, c * XT:(c + 1) * XT, :]).then_inc(x_landed[c], DMA)
                if c == 0:
                    sp.dma_start(w_sb[:, :, :], w.rearrange("(k p) n -> p k n", p=P)).then_inc(w_landed, DMA)

            for n in range(NT):
                s = n % TG
                if n >= TG:
                    sp.wait_ge(quarter_summed, QA * (n - TG + 1))
                    sp.wait_ge(last_summed, QA * (n - TG + 1))
                    sp.wait_ge(diag_copied, n - TG + 1)
                    if n >= 2 * TG:
                        sp.wait_ge(at_ready, left_end(n - TG))
                for q in range(QN):
                    sp.dma_start(natural[s][q * R:(q + 1) * R, :, :],
                                 adj_rows[n, :, :, q * SPAN:(q + 1) * SPAN]).then_inc(natural_landed[s], DMA)
            sp.dma_start(b_sb[:, :], b.partition_broadcast(P)).then_inc(b_landed, DMA)

            def load_right(u):
                T, s, rows = loads[u]
                for i in range(rows):
                    for q in range(QN):
                        sp.dma_start(right_part(u % TG, i, T)[q * R:(q + 1) * R],
                                     adj_rows[TG * T + s + i, :, :, q * SPAN + GW * (T + 1):(q + 1) * SPAN]
                                     ).then_inc(natural_landed[u % TG], DMA)

            def load_x(k):
                for q in range(QN):
                    sp.dma_start(x_again[q * R:(q + 1) * R, k % TG, :], x_rows[q, :, place(k), :]).then_inc(
                        x_again_landed[k % TG], DMA)

            def store(k):
                sp.wait_ge(result_ready, k + 1)
                for q in range(QN):
                    sp.dma_start(out_rows[place(k), q], result[k % TG][q * R:(q + 1) * R, :]).then_inc(
                        stored[k % TG], DMA)
                if k + TG < NT:
                    load_x(k + TG)

            k = 0
            for u in range(len(loads)):
                free = left_end(NT - TG + u) if u < TG else load_end(u - TG)
                for k in range(k, finished(free - 1)):
                    store(k)
                k = finished(free - 1)
                if u < TG:
                    sp.wait_ge(quarter_summed, QA * (NT - TG + u + 1))
                    sp.wait_ge(last_summed, QA * (NT - TG + u + 1))
                    sp.wait_ge(diag_copied, NT - TG + u + 1)
                sp.wait_ge(at_ready, free)
                load_right(u)
                if u == 1:
                    sp.wait_ge(quarter_summed, QA * NT)
                    for f in range(TG):
                        load_x(f)
            for k in range(k, NT):
                store(k)
            for s in range(TG):
                sp.wait_ge(stored[s], QN * DMA * (NT // TG))

        @block.scalar
        def _(act):
            def sum_quarter(n, q):
                if q == 0:
                    act.wait_ge(natural_landed[n % TG], QN * DMA * (n // TG + 1))
                if q == 0:
                    at_least(act, quarter_summed, QA * n)
                elif q == 1:
                    at_least(act, last_summed, QA * min(n, SUMMED))
                else:
                    act.wait_ge(quarter_summed, QA * n + q - 1)
                nc.scalar.activation(junk[q % 2], natural[n % TG][:, q, :], ACT.Copy,
                                     accum_out=part_sum[:, n, q:q + 1]).then_inc(
                                         *((quarter_summed, 1) if q < QA else (last_summed, QA)))

            def take_hw(t):
                if t % XT == 0:
                    act.wait_ge(rstd_ready, t // XT + 1)
                act.wait_ge(hw_made, t + 1)
                nc.scalar.activation(acc[:, t, :], bank[:, t % AR, 0:D], ACT.Copy,
                                     scale=rstd[:, t:t + 1]).then_inc(hw_ready, 1)

            def round_group(k):
                act.wait_ge(at_ready, k + 1)
                at_least(act, group_used, k - RING + 1)
                nc.scalar.copy(hi[k % RING][:, :, :], at[k % RING][:, :, :]).then_inc(hi_ready, 1)

            for t in range(FIRST_TAKES):
                take_hw(t)
            for n in range(SUMMED):
                for q in range(QN):
                    take_hw(FIRST_TAKES + QN * n + q)
                    sum_quarter(n, q)

            k = 0
            for n in range(NT):
                T, s = divmod(n, TG)
                quarters = list(range(QA)) if SUMMED <= n + 1 < NT else []
                for g in range(T):
                    round_group(k)
                    k += 1
                    if T >= BUSY and quarters:
                        sum_quarter(n + 1, quarters.pop(0))
                if s == TG - 1:
                    for j in range(TG):
                        round_group(k)
                        k += 1
                for q in quarters:
                    sum_quarter(n + 1, q)
            for k in range(k, right_groups(-1)):
                round_group(k)

        @block.gpsimd
        def _(pool):
            step = [0]

            def then(ins):
                step[0] += 1
                ins.then_inc(pool_step, 1)
                pool.wait_ge(pool_step, step[0])

            then(nc.gpsimd.memset(minus_half[:, :], -0.5))
            then(nc.gpsimd.memset(ident[:, :], 0.0))
            then(nc.gpsimd.memset(same_r[:, :], 0.0))
            then(nc.gpsimd.memset(own_q[:, :], 0.0))
            then(nc.gpsimd.affine_select(out=ident[:, :], in_=ident[:, :], compare_op=ALU.not_equal, fill=1.0,
                                         base=0, pattern=[[-1, P]], channel_multiplier=1))
            for q in range(QN):
                v = same_r[:, :].rearrange("p (a r) -> p a r", a=QN)
                then(nc.gpsimd.affine_select(out=v, in_=v, compare_op=ALU.not_equal, fill=1.0,
                                             base=-q * R, pattern=[[0, QN], [-1, R]], channel_multiplier=1))
                then(nc.gpsimd.memset(own_q[q * R:(q + 1) * R, q:q + 1], 1.0))
            pool.sem_inc(consts_made, 1)

            for c in range(XP):
                pool.wait_ge(var_ready, c + 1)
                nc.gpsimd.tensor_tensor(out=rstd[:, c * XT:(c + 1) * XT], in0=var[:, c * XT:(c + 1) * XT],
                                        in1=minus_half[:, :], op=ALU.pow).then_inc(rstd_ready, 1)

            def subtract(k, slot):
                pool.wait_ge(hi_ready, k + 1)
                at_least(pool, group_used, k - RING + 1)
                nc.gpsimd.tensor_tensor(out=lo[slot][:, SPLIT:, :], in0=at[slot][:, SPLIT:, :],
                                        in1=hi[slot][:, SPLIT:, :].bitcast(F32),
                                        op=ALU.subtract).then_inc(lo_ready2, 1)

            for s in range(TG):
                pool.wait_ge(natural_landed[s], QN * DMA)
                nc.gpsimd.tensor_copy(diag[s][:, :, :], natural[s][:, :, 0:GW]).then_inc(diag_copied, 1)
            for T in range(NS):
                for i, (s, j0) in enumerate(rows_of(pool, T)):
                    n = TG * T + s
                    for g in range(max(T, 1)):
                        if g < T:
                            subtract(left_groups(T) + s * T + g, (j0 + g) % RING)
                        if g == min(1, max(T - 1, 0)):
                            pool.wait_ge(sum_ready, n + 1)
                            nc.gpsimd.tensor_tensor(out=row_pow[:, :], in0=row_safe[i % 2][:, :],
                                                    in1=minus_half[:, 0:1], op=ALU.pow).then_inc(pow_done, 1)
                            pool.wait_ge(pow_done, n + 1)
                            nc.gpsimd.tensor_tensor(out=d[:, bass.ds(n, 1)], in0=row_pow[:, :],
                                                    in1=row_pos[i % 2][:, :], op=ALU.mult).then_inc(d_ready, 1)
                for j in range(TG):
                    subtract(left_groups(T) + TG * T + j, j)
            for T in reversed(range(NS - 1)):
                W = NS - 1 - T
                for s, j0 in rows_of(pool, W):
                    for g in range(W):
                        subtract(right_groups(T) + s * W + g, (j0 + g) % RING)

        @block.vector
        def _(dve):
            def moments(c):
                tiles = slice(c * XT, (c + 1) * XT)
                before = c * (XT + 2)
                dve.wait_ge(x_landed[c], QN * DMA)
                for t in range(c * XT, (c + 1) * XT):
                    nc.vector.bn_stats(stats[:, t, :], acc[:, t, :]).then_inc(stats_step, 1)
                dve.wait_ge(stats_step, before + XT)
                st = stats[:, tiles, :]
                nc.vector.tensor_tensor(out=mean2[:, :], in0=st[:, :, 1], in1=st[:, :, 4], op=ALU.add)
                nc.vector.tensor_tensor(out=mean_dif[:, :], in0=st[:, :, 1], in1=st[:, :, 4], op=ALU.subtract)
                nc.vector.tensor_tensor(out=m2[:, :], in0=st[:, :, 2], in1=st[:, :, 5],
                                        op=ALU.add).then_inc(stats_step, 1)
                dve.wait_ge(stats_step, before + XT + 1)
                nc.vector.tensor_scalar(mean[:, tiles], mean2[:, :], 0.5, None, ALU.mult).then_inc(mean_ready, 1)
                nc.vector.tensor_tensor(out=mean_dif2[:, :], in0=mean_dif[:, :], in1=mean_dif[:, :], op=ALU.mult)
                nc.vector.tensor_scalar(m2_eps[:, :], m2[:, :], 1.0 / D, EPS, ALU.mult,
                                        ALU.add).then_inc(stats_step, 1)
                dve.wait_ge(stats_step, before + XT + 2)
                nc.vector.scalar_tensor_tensor(out=var[:, tiles], in0=mean_dif2[:, :], scalar=0.25,
                                               in1=m2_eps[:, :], op0=ALU.mult, op1=ALU.add).then_inc(var_ready, 1)

            def centre(i):
                for j in range(AR):
                    t = AR * i + j
                    at_least(dve, hT_made, t - AR + 1)
                    nc.vector.tensor_scalar(centred[j], acc[:, t, :], mean[:, bass.ds(t, 1)],
                                            0.0, ALU.subtract, ALU.max).then_inc(centred_ready, 1)

            def move_hT(i):
                for j in range(AR):
                    t = AR * i + j
                    dve.wait_ge(hT_made, t + 1)
                    at_least(dve, hw_made, t - AR + 1)
                    nc.vector.tensor_copy(hT[j], ps_hT[j][:, 0:D]).then_inc(hT_ready, 1)

            moments(0)
            dve.wait_ge(mean_ready, 1)
            centre(0)
            centre(1)
            move_hT(0)
            for c in range(1, XP):
                moments(c)
                dve.wait_ge(mean_ready, c + 1)
                with dve.Fori(c * XT // AR, (c + 1) * XT // AR) as i:
                    centre(i)
                    move_hT(i - 1)
            move_hT(NT // AR - 1)

            def subtract(k):
                slot = k % RING
                dve.wait_ge(hi_ready, k + 1)
                at_least(dve, group_used, k - RING + 1)
                nc.vector.tensor_tensor(out=lo[slot][:, 0:SPLIT, :], in0=at[slot][:, 0:SPLIT, :],
                                        in1=hi[slot][:, 0:SPLIT, :].bitcast(F32),
                                        op=ALU.subtract).then_inc(lo_ready, 1)

            def move(k, src):
                at_least(dve, lo_ready, k - RING + 1)
                at_least(dve, lo_ready2, k - RING + 1)
                nc.vector.transpose(at[k % RING][:, :, :].rearrange("p t (q r) -> p q t r", q=QN),
                                    src.rearrange("p q (t c) -> p q t c", c=R)).then_inc(at_ready, 1)

            def row_sums(n):
                dve.wait_ge(sum_made, n + 1)
                nc.vector.tensor_tensor_reduce(
                    out=own_part[:, :], in0=ps_sum[n % 2][:, 0:QN], in1=own_q[:, :], scale=1.0,
                    scalar=0.0, op0=ALU.mult, op1=ALU.add,
                    accum_out=row_sum[:, :]).then_inc(own_summed, 1)
                dve.wait_ge(own_summed, n + 1)
                at_least(dve, d_ready, n - 1)
                nc.vector.tensor_scalar(row_safe[n % 2][:, :], row_sum[:, :], TINY, None, ALU.max)
                nc.vector.tensor_scalar(row_pos[n % 2][:, :], row_sum[:, :], 0.0, None,
                                        ALU.is_gt).then_inc(sum_ready, 1)

            dve.wait_ge(consts_made, 1)
            dve.wait_ge(hw_ready, NT)
            dve.wait_ge(diag_copied, TG)
            dve.wait_ge(last_summed, QA * SUMMED)
            k = 0
            for n in range(NT):
                T, s = divmod(n, TG)
                if n >= TG:
                    dve.wait_ge(natural_landed[s], QN * DMA * (T + 1))
                    at_least(dve, at_ready, left_groups(T - 1) + TG * (T - 1) + s + 1)
                    nc.vector.tensor_copy(diag[s][:, :, :],
                                          natural[s][:, :, T * GW:(T + 1) * GW]).then_inc(diag_copied, 1)
                if n >= SUMMED:
                    nc.vector.tensor_reduce(out=part_sum[:, n, QA:QN], in_=natural[s][:, QA, :], op=ALU.add,
                                            axis=AX.X).then_inc(last_summed, QA)
                if T >= 1:
                    dve.wait_ge(group_used, left_groups(T) - TG + s + 1)
                    nc.vector.tensor_copy(hi_total, bank[:, s, 0:D]).then_inc(hi_totalled, 1)
                    dve.wait_ge(hi_totalled, n - TG + 1)
                    nc.vector.tensor_tensor(out=acc[:, n - TG, :], in0=hi_total, in1=bank[:, s, D:2 * D],
                                            op=ALU.add).then_inc(acc_saved, 1)
                if T == 0:
                    row_sums(n)
                for g in range(T):
                    move(k, natural[s][:, :, g * GW:(g + 1) * GW])
                    if g > 0 or s > 0 and T >= BUSY:
                        subtract(k - 1)
                    k += 1
                    if g == min(1, T - 1):
                        row_sums(n)
                if 0 < T < BUSY or T and s == TG - 1:
                    subtract(k - 1)
                dve.wait_ge(d_ready, n + 1)
                nc.vector.tensor_scalar(G[:, n, 0, :], acc[:, n, :], d[:, n:n + 1], None,
                                        ALU.mult).then_inc(G_hi_made, 1)
                dve.wait_ge(G_hi_made, n + 1)
                nc.vector.scalar_tensor_tensor(
                    out=G[:, n, 1, :], in0=acc[:, n, :], scalar=d[:, n:n + 1],
                    in1=G[:, n, 0, :].bitcast(F32), op0=ALU.mult, op1=ALU.subtract).then_inc(G_ready, 1)
                if s == TG - 1:
                    for j in range(TG):
                        move(k, diag[j][:, :, :])
                        if j > 0:
                            subtract(k - 1)
                        k += 1
                    subtract(k - 1)

            def finish(k):
                t, s = place(k), k % TG
                dve.wait_ge(group_used, group_end(k))
                if k < TG:
                    nc.vector.tensor_copy(hi_total, bank[:, s, 0:D]).then_inc(hi_totalled, 1)
                else:
                    nc.vector.tensor_tensor(out=hi_total, in0=bank[:, s, 0:D], in1=acc[:, t, :],
                                            op=ALU.add).then_inc(hi_totalled, 1)
                dve.wait_ge(hi_totalled, NT - TG + k + 1)
                nc.vector.tensor_tensor(out=total, in0=bank[:, s, D:2 * D], in1=hi_total,
                                        op=ALU.add).then_inc(bank_taken, 1)
                dve.wait_ge(bank_taken, k + 1)
                at_least(dve, stored[s], QN * DMA * (k // TG))
                nc.vector.scalar_tensor_tensor(out=result[s][:, :], in0=total, scalar=d[:, t:t + 1],
                                               in1=b_sb[:, :], op0=ALU.mult, op1=ALU.add).then_inc(biased_ready, 1)
                dve.wait_ge(biased_ready, k + 1)
                dve.wait_ge(x_again_landed[s], QN * DMA * (k // TG + 1))
                nc.vector.scalar_tensor_tensor(out=result[s][:, :], in0=result[s][:, :], scalar=0.0,
                                               in1=x_again[:, s, :], op0=ALU.max, op1=ALU.add).then_inc(result_ready, 1)

            dve.wait_ge(acc_saved, NT - TG)
            dve.wait_ge(b_landed, DMA)
            landed = [NT // TG] * TG
            for u, (T, s0, rows) in enumerate(loads):
                slot = u % TG
                landed[slot] += rows
                dve.wait_ge(natural_landed[slot], QN * DMA * landed[slot])
                for i in range(rows):
                    for g in range(NS - 1 - T):
                        move(k, right_part(slot, i, T)[:, :, g * GW:(g + 1) * GW])
                        if k > left_groups(NS):
                            subtract(k - 1)
                        k += 1
                        for f in range(finished(k - 1), finished(k)):
                            finish(f)
            subtract(k - 1)
            for f in range(finished(k), NT):
                finish(f)

        @block.tensor
        def _(pe):
            def transpose_rows(i):
                for j in range(AR):
                    t = AR * i + j
                    pe.wait_ge(centred_ready, t + 1)
                    at_least(pe, hT_ready, t - AR + 1)
                    for f in range(KD):
                        last = nc.tensor.transpose(ps_hT[j][:, f * P:(f + 1) * P], centred[j][:, f * P:(f + 1) * P],
                                                   ident[:, :])
                    last.then_inc(hT_made, 1)

            def project(i):
                for j in range(AR):
                    t = AR * i + j
                    pe.wait_ge(hT_ready, t + 1)
                    at_least(pe, hw_ready, t - AR + 1)
                    for f in range(KD):
                        last = nc.tensor.matmul(bank[:, j, 0:D], hT[j][:, f * P:(f + 1) * P], w_sb[:, f, :],
                                                start=(f == 0), stop=(f == KD - 1))
                    last.then_inc(hw_made, 1)

            pe.wait_ge(consts_made, 1)
            pe.wait_ge(w_landed, DMA)
            transpose_rows(0)
            transpose_rows(1)
            project(0)
            with pe.Fori(1, NT // AR - 1) as i:
                transpose_rows(i + 1)
                project(i)
            project(NT // AR - 1)

            def multiply(k, slot, s, g, first, last):
                pe.wait_ge(hi_ready, k + 1)
                for j in range(TG):
                    nc.tensor.matmul(bank[:, s, :], hi[slot][:, j, :],
                                     G[:, g * TG + j, :, :].rearrange("p a f -> p (a f)"),
                                     start=(first and j == 0), stop=False)
                pe.wait_ge(lo_ready, k + 1)
                for j in range(TG):
                    if j == SPLIT:
                        pe.wait_ge(lo_ready2, k + 1)
                    mm = nc.tensor.matmul(bank[:, s, D:2 * D], lo[slot][:, j, :], G[:, g * TG + j, 0, :],
                                          start=False, stop=(last and j == TG - 1))
                mm.then_inc(group_used, 1)

            pe.wait_ge(hw_ready, NT)
            pe.wait_ge(hT_ready, NT)
            for T in range(NS):
                for i, (s, j0) in enumerate(rows_of(pe, T)):
                    n = TG * T + s
                    pe.wait_ge(quarter_summed, QA * (n + 1))
                    pe.wait_ge(last_summed, QA * (n + 1))
                    at_least(pe, own_summed, n - 1)
                    nc.tensor.matmul(ps_sum[i % 2][:, 0:QN], same_r[:, :], part_sum[:, n, :],
                                     start=True, stop=True).then_inc(sum_made, 1)
                    if T >= 1:
                        pe.wait_ge(acc_saved, n - TG + 1)
                    for g in range(T):
                        multiply(left_groups(T) + s * T + g, (j0 + g) % RING, s, g, g == 0, False)
                pe.wait_ge(G_ready, TG * (T + 1))
                for s in range(TG):
                    multiply(left_groups(T) + TG * T + s, s, s, T, T == 0, True)
            for T in reversed(range(NS - 1)):
                W = NS - 1 - T
                for s, j0 in rows_of(pe, W):
                    pe.wait_ge(bank_taken, TG * (W - 1) + s + 1)
                    for g in range(W):
                        multiply(right_groups(T) + s * W + g, (j0 + g) % RING, s, T + 1 + g, g == 0, g == W - 1)


INPUTS = ["x", "adj", "L0_gnn_W", "L0_gnn_b"]


def kernel(**inputs):
    import concourse.bacc as bacc
    from concourse.bass_utils import run_bass_kernel_spmd

    nc = bacc.Bacc("TRN2", target_bir_lowering=False, num_devices=1)
    arrays, args = {}, []
    for name in INPUTS:
        a = np.ascontiguousarray(inputs[name])
        arrays[f"in_{name}"] = a
        args.append(nc.dram_tensor(f"in_{name}", a.shape, mybir.dt.from_np(a.dtype), kind="ExternalInput").ap())
    out = nc.dram_tensor("out", arrays["in_x"].shape, F32, kind="ExternalOutput").ap()
    build(nc, *args, out)
    r = run_bass_kernel_spmd(nc, [arrays], core_ids=[0])
    return r.results[0]["out"]
```

```python
from contextlib import ExitStack

import numpy as np

import concourse.bass as bass
from concourse import mybir

ALU = mybir.AluOpType
ACT = mybir.ActivationFunctionType
AX = mybir.AxisListType
F32 = mybir.dt.float32
BF16 = mybir.dt.bfloat16
F32R = mybir.dt.float32r

P = 128
QN = 4
R = 32
BANK = 512
DMA = 16
EPS = 1e-5
TINY = float(np.finfo(np.float32).tiny)


def at_least(eng, sem, value):
    if not isinstance(value, int) or value > 0:
        eng.wait_ge(sem, value)


def build(nc, x, adj, w, b, out):
    N, D = x.shape
    SPAN = N // QN
    NT = SPAN // R
    TG = 4
    NS = NT // TG
    GW = TG * R
    KD = D // P
    XP = 4
    XT = NT // XP
    AR = 4
    RING = 4
    SUMMED = 5
    WHOLE = 3
    QA = QN - 1
    FIRST_TAKES = 6
    SPLIT = 1
    BUSY = 5
    D_AT = 2
    LAG = 4

    adj_rows = adj.rearrange("(q t r) c -> t r q c", q=QN, r=R)
    x_rows = x.rearrange("(q t r) f -> q r t f", q=QN, r=R)
    out_rows = out.rearrange("(q t r) f -> t q r f", q=QN, r=R)

    def left_groups(T):
        return TG * (T * (T - 1) // 2 + T)

    def left_end(n):
        T, s = divmod(n, TG)
        return left_groups(T) + (s + 1) * T

    PAIRS = TG * (NS - 1) // 2

    def pair(u):
        i, s = divmod(u, TG)
        if i < NS // 2 - 1:
            return (NS - 2 - i, s), (i, s)
        return (i, 2 * s), (i, 2 * s + 1)

    def right_groups(u):
        return left_groups(NS) + NS * u

    def place(k):
        if k < TG:
            return NT - TG + k
        T, s = pair((k - TG) // 2)[k % 2]
        return TG * T + s

    def group_end(k):
        if k < TG:
            return left_groups(NS) - TG + k + 1
        u = (k - TG) // 2
        return right_groups(u + 1) if k % 2 else right_groups(u) + NS - 1 - pair(u)[0][0]

    def finished(groups):
        return sum(group_end(k) + LAG <= groups for k in range(NT)) if groups > left_groups(NS) else 0

    with ExitStack() as ctx:
        def sb(name, shape, dt=F32):
            return ctx.enter_context(nc.sbuf_tensor(name, shape, dt))

        def ps(name, shape):
            return ctx.enter_context(nc.psum_tensor(name, shape, F32))

        def sem(name):
            return ctx.enter_context(nc.semaphore(name))

        w_sb = sb("w_sb", [P, KD, D])
        b_sb = sb("b_sb", [P, D])
        ident = sb("ident", [P, P])
        same_r = sb("same_r", [P, P])
        own_q = sb("own_q", [P, QN])
        minus_half = sb("minus_half", [P, XT])
        stats = sb("stats", [P, NT, 6])
        mean2 = sb("mean2", [P, XT])
        mean_dif = sb("mean_dif", [P, XT])
        mean_dif2 = sb("mean_dif2", [P, XT])
        m2 = sb("m2", [P, XT])
        m2_eps = sb("m2_eps", [P, XT])
        mean = sb("mean", [P, NT])
        var = sb("var", [P, NT])
        rstd = sb("rstd", [P, NT])
        natural = [sb(f"natural{s}", [P, QN, SPAN]) for s in range(TG)]
        diag = [sb(f"diag{s}", [P, TG, P]) for s in range(TG)]
        at = [sb(f"at{k}", [P, TG, P]) for k in range(RING)]
        hi = [sb(f"hi{k}", [P, TG, P], F32R) for k in range(RING)]
        lo = [sb(f"lo{k}", [P, TG, P], F32R) for k in range(RING)]
        part_sum = sb("part_sum", [P, NT, QN])
        own_part = sb("own_part", [P, QN])
        row_sum = sb("row_sum", [P, 1])
        row_safe = [sb(f"row_safe{e}", [P, 1]) for e in range(2)]
        row_pos = [sb(f"row_pos{e}", [P, 1]) for e in range(2)]
        row_pow = [sb(f"row_pow{e}", [P, 1]) for e in range(2)]
        d = sb("d", [P, NT])
        G = sb("G", [P, NT, 2, D], F32R)
        acc = sb("acc", [P, NT, D])
        x_again = sb("x_again", [P, TG, D])
        result = [sb(f"result{s}", [P, D]) for s in range(TG)]

        def half(k, i):
            return at[k][:, 2 * i:2 * i + 2, :].rearrange("p t r -> p (t r)")

        centred = [half(j // 2, j % 2) for j in range(AR)]
        hT = [half(2 + j // 2, j % 2) for j in range(AR)]
        hi_total, total = w_sb[:, 0, :], w_sb[:, 1, :]
        junk = [x_again[:, 2 * i:2 * i + 2, :].rearrange("p s f -> p (s f)").bitcast(BF16) for i in range(2)]

        bank = ps("bank", [P, TG, BANK])
        ps_hT = [ps(f"ps_hT{j}", [P, BANK]) for j in range(AR)]
        ps_sum = ps_hT

        x_landed = [sem(f"x_landed{c}") for c in range(XP)]
        x_again_landed = [sem(f"x_again_landed{s}") for s in range(TG)]
        w_landed = sem("w_landed")
        b_landed = sem("b_landed")
        consts_made = sem("consts_made")
        stats_made = sem("stats_made")
        mean_ready = sem("mean_ready")
        rstd_ready = sem("rstd_ready")
        centred_ready = sem("centred_ready")
        hT_made = sem("hT_made")
        hT_ready = sem("hT_ready")
        hw_made = sem("hw_made")
        hw_ready = sem("hw_ready")
        natural_landed = [sem(f"natural_landed{s}") for s in range(TG)]
        quarter_summed = sem("quarter_summed")
        last_summed = sem("last_summed")
        diag_moved = sem("diag_moved")
        sum_made = sem("sum_made")
        own_summed = sem("own_summed")
        sum_ready = sem("sum_ready")
        pow_done = sem("pow_done")
        d_ready = sem("d_ready")
        G_ready = sem("G_ready")
        at_ready = sem("at_ready")
        hi_ready = sem("hi_ready")
        lo_ready = sem("lo_ready")
        lo_ready2 = sem("lo_ready2")
        group_used = sem("group_used")
        G_hi_made = sem("G_hi_made")
        hi_saved = sem("hi_saved")
        acc_saved = sem("acc_saved")
        hi_totalled = sem("hi_totalled")
        bank_taken = sem("bank_taken")
        biased_ready = sem("biased_ready")
        result_ready = sem("result_ready")
        stored = [sem(f"stored{s}") for s in range(TG)]
        pool_step = sem("pool_step")

        block = ctx.enter_context(nc.Block())

        def rows_of(eng, groups):
            if groups and 2 * groups % RING == 0:
                with eng.Fori(0, 2) as h:
                    for e in range(2):
                        yield 2 * h + e, e * groups
            else:
                for s in range(TG):
                    yield s, s * groups

        def at_free(k, i):
            return k - (2 * RING if i < TG else RING) + 1

        def right_part(slot, first, W):
            flat = natural[slot][:, :, :].rearrange("p q c -> p (q c)")
            return flat[:, first * QN * GW:(first + W) * QN * GW].rearrange("p (q c) -> p q c", q=QN)

        def looped_pairs(eng):
            for i in range(NS // 2):
                if i < NS // 2 - 1:
                    with eng.Fori(0, 2) as h:
                        for e in range(2):
                            yield TG * i + 2 * h + e, TG * i + e, e
                else:
                    for e in range(2):
                        yield TG * i + e, TG * i + e, e

        @block.sync
        def _(sp):
            for c in range(XP):
                for q in range(QN):
                    sp.dma_start(acc[q * R:(q + 1) * R, c * XT:(c + 1) * XT, :],
                                 x_rows[q, :, c * XT:(c + 1) * XT, :]).then_inc(x_landed[c], DMA)
                if c == 0:
                    sp.dma_start(w_sb[:, :, :], w.rearrange("(k p) n -> p k n", p=P)).then_inc(w_landed, DMA)

            for n in range(NT):
                s = n % TG
                if n >= TG:
                    sp.wait_ge(quarter_summed, QA * (n - TG + 1))
                    sp.wait_ge(last_summed, QA * (n - TG + 1))
                    sp.wait_ge(diag_moved, n - TG + 1)
                    if n >= 2 * TG:
                        sp.wait_ge(at_ready, left_end(n - TG) - TG * (n // TG - 1))
                for q in range(QN):
                    sp.dma_start(natural[s][q * R:(q + 1) * R, :, :],
                                 adj_rows[n, :, :, q * SPAN:(q + 1) * SPAN]).then_inc(natural_landed[s], DMA)
            sp.dma_start(b_sb[:, :], b.partition_broadcast(P)).then_inc(b_landed, DMA)

            def load_pair(u):
                first = 0
                for T, s in pair(u):
                    W = NS - 1 - T
                    for q in range(QN):
                        sp.dma_start(right_part(u % TG, first, W)[q * R:(q + 1) * R],
                                     adj_rows[TG * T + s, :, :, q * SPAN + GW * (T + 1):(q + 1) * SPAN]
                                     ).then_inc(natural_landed[u % TG], DMA)
                    first += W

            def load_x(k):
                for q in range(QN):
                    sp.dma_start(x_again[q * R:(q + 1) * R, k % TG, :], x_rows[q, :, place(k), :]).then_inc(
                        x_again_landed[k % TG], DMA)

            def store(k):
                sp.wait_ge(result_ready, k + 1)
                for q in range(QN):
                    sp.dma_start(out_rows[place(k), q], result[k % TG][q * R:(q + 1) * R, :]).then_inc(
                        stored[k % TG], DMA)
                if k + TG < NT:
                    load_x(k + TG)

            k = 0
            for u in range(PAIRS):
                free = left_end(NT - TG + u) if u < TG else right_groups(u - TG + 1)
                diagonal = NT - TG if u < TG else NT
                for k in range(k, finished(free - 1)):
                    store(k)
                k = finished(free - 1)
                if u < TG:
                    sp.wait_ge(quarter_summed, QA * (NT - TG + u + 1))
                    sp.wait_ge(last_summed, QA * (NT - TG + u + 1))
                    sp.wait_ge(diag_moved, NT - TG + u + 1)
                sp.wait_ge(at_ready, free - diagonal)
                load_pair(u)
                if u == 1:
                    sp.wait_ge(quarter_summed, QA * NT)
                    for f in range(TG):
                        load_x(f)
            for k in range(k, NT):
                store(k)
            for s in range(TG):
                sp.wait_ge(stored[s], QN * DMA * (NT // TG))

        @block.scalar
        def _(act):
            def sum_quarter(n, q):
                if q == 0:
                    act.wait_ge(natural_landed[n % TG], QN * DMA * (n // TG + 1))
                if q == 0:
                    at_least(act, quarter_summed, QA * n)
                elif q == 1:
                    at_least(act, last_summed, QA * min(n, WHOLE))
                else:
                    act.wait_ge(quarter_summed, QA * n + q - 1)
                nc.scalar.activation(junk[q % 2], natural[n % TG][:, q, :], ACT.Copy,
                                     accum_out=part_sum[:, n, q:q + 1]).then_inc(
                                         *((quarter_summed, 1) if q < QA else (last_summed, QA)))

            def take_hw(t):
                if t % XT == 0:
                    act.wait_ge(rstd_ready, t // XT + 1)
                act.wait_ge(hw_made, t + 1)
                nc.scalar.activation(acc[:, t, :], bank[:, t % AR, 0:D], ACT.Copy,
                                     scale=rstd[:, t:t + 1]).then_inc(hw_ready, 1)

            def round_group(k, diagonal):
                act.wait_ge(at_ready, k - diagonal + 1)
                at_least(act, group_used, k - RING + 1)
                nc.scalar.copy(hi[k % RING][:, :, :], at[k % RING][:, :, :]).then_inc(hi_ready, 1)

            def round_diag(k, n):
                act.wait_ge(diag_moved, n + 1)
                at_least(act, group_used, k - RING + 1)
                nc.scalar.copy(hi[k % RING][:, :, :], diag[n % TG][:, :, :]).then_inc(hi_ready, 1)

            for t in range(FIRST_TAKES):
                take_hw(t)
            t = FIRST_TAKES
            for n in range(SUMMED):
                for q in range(QN if n < WHOLE else QA):
                    take_hw(t)
                    t += 1
                    sum_quarter(n, q)
            for t in range(t, NT):
                take_hw(t)

            k = 0
            for n in range(NT):
                T, s = divmod(n, TG)
                if T >= 1:
                    act.wait_ge(group_used, left_groups(T) - TG + s + 1)
                    nc.scalar.copy(acc[:, n - TG, :], bank[:, s, 0:D]).then_inc(hi_saved, 1)
                quarters = list(range(QA)) if SUMMED <= n + 1 < NT else []
                for g in range(T):
                    round_group(k, TG * T)
                    k += 1
                    if T >= BUSY and quarters:
                        sum_quarter(n + 1, quarters.pop(0))
                if s == TG - 1:
                    for j in range(TG):
                        round_diag(k, TG * T + j)
                        k += 1
                for q in quarters:
                    sum_quarter(n + 1, q)
            for k in range(k, right_groups(PAIRS)):
                round_group(k, NT)

        @block.gpsimd
        def _(pool):
            step = [0]

            def then(ins):
                step[0] += 1
                ins.then_inc(pool_step, 1)
                pool.wait_ge(pool_step, step[0])

            then(nc.gpsimd.memset(minus_half[:, :], -0.5))
            then(nc.gpsimd.memset(ident[:, :], 0.0))
            then(nc.gpsimd.memset(same_r[:, :], 0.0))
            then(nc.gpsimd.memset(own_q[:, :], 0.0))
            then(nc.gpsimd.affine_select(out=ident[:, :], in_=ident[:, :], compare_op=ALU.not_equal, fill=1.0,
                                         base=0, pattern=[[-1, P]], channel_multiplier=1))
            for q in range(QN):
                v = same_r[:, :].rearrange("p (a r) -> p a r", a=QN)
                then(nc.gpsimd.affine_select(out=v, in_=v, compare_op=ALU.not_equal, fill=1.0,
                                             base=-q * R, pattern=[[0, QN], [-1, R]], channel_multiplier=1))
                then(nc.gpsimd.memset(own_q[q * R:(q + 1) * R, q:q + 1], 1.0))
            pool.sem_inc(consts_made, 1)

            for c in range(XP):
                tiles = slice(c * XT, (c + 1) * XT)
                st = stats[:, tiles, :]
                pool.wait_ge(stats_made, (c + 1) * XT)
                then(nc.gpsimd.tensor_tensor(out=mean2[:, :], in0=st[:, :, 1], in1=st[:, :, 4], op=ALU.add))
                nc.gpsimd.tensor_scalar(mean[:, tiles], mean2[:, :], 0.5, None, ALU.mult).then_inc(mean_ready, 1)
                then(nc.gpsimd.tensor_tensor(out=mean_dif[:, :], in0=st[:, :, 1], in1=st[:, :, 4], op=ALU.subtract))
                nc.gpsimd.tensor_tensor(out=m2[:, :], in0=st[:, :, 2], in1=st[:, :, 5], op=ALU.add)
                then(nc.gpsimd.tensor_tensor(out=mean_dif2[:, :], in0=mean_dif[:, :], in1=mean_dif[:, :], op=ALU.mult))
                nc.gpsimd.tensor_scalar(m2_eps[:, :], m2[:, :], 1.0 / D, EPS, ALU.mult, ALU.add)
                then(nc.gpsimd.tensor_scalar(mean_dif2[:, :], mean_dif2[:, :], 0.25, None, ALU.mult))
                then(nc.gpsimd.tensor_tensor(out=var[:, tiles], in0=mean_dif2[:, :], in1=m2_eps[:, :], op=ALU.add))
                nc.gpsimd.tensor_tensor(out=rstd[:, tiles], in0=var[:, tiles],
                                        in1=minus_half[:, :], op=ALU.pow).then_inc(rstd_ready, 1)

            def subtract(k, slot, src):
                pool.wait_ge(hi_ready, k + 1)
                at_least(pool, group_used, k - RING + 1)
                nc.gpsimd.tensor_tensor(out=lo[slot][:, SPLIT:, :], in0=src[slot][:, SPLIT:, :],
                                        in1=hi[slot][:, SPLIT:, :].bitcast(F32),
                                        op=ALU.subtract).then_inc(lo_ready2, 1)

            for T in range(NS):
                for i, (s, j0) in enumerate(rows_of(pool, T)):
                    n = TG * T + s
                    for g in range(max(T, 1)):
                        if g < T:
                            subtract(left_groups(T) + s * T + g, (j0 + g) % RING, at)
                        if g == min(D_AT, max(T - 1, 0)):
                            at_least(pool, d_ready, n - 1)
                            pool.wait_ge(sum_ready, n + 1)
                            nc.gpsimd.tensor_tensor(out=row_pow[i % 2][:, :], in0=row_safe[i % 2][:, :],
                                                    in1=minus_half[:, 0:1], op=ALU.pow).then_inc(pow_done, 1)
                            pool.wait_ge(pow_done, n + 1)
                            nc.gpsimd.tensor_tensor(out=d[:, bass.ds(n, 1)], in0=row_pow[i % 2][:, :],
                                                    in1=row_pos[i % 2][:, :], op=ALU.mult).then_inc(d_ready, 1)
                for j in range(TG):
                    subtract(left_groups(T) + TG * T + j, j, diag)
            for u, _, _ in looped_pairs(pool):
                for j in range(NS):
                    subtract(right_groups(u) + j, j % RING, at)

        @block.vector
        def _(dve):
            def moments(i):
                for j in range(AR):
                    t = AR * i + j
                    nc.vector.bn_stats(stats[:, t, :], acc[:, t, :]).then_inc(stats_made, 1)

            def centre(i):
                for j in range(AR):
                    t = AR * i + j
                    at_least(dve, hT_made, t - AR + 1)
                    nc.vector.tensor_scalar(centred[j], acc[:, t, :], mean[:, bass.ds(t, 1)],
                                            0.0, ALU.subtract, ALU.max).then_inc(centred_ready, 1)

            def move_hT(i):
                for j in range(AR):
                    t = AR * i + j
                    dve.wait_ge(hT_made, t + 1)
                    at_least(dve, hw_made, t - AR + 1)
                    nc.vector.tensor_copy(hT[j], ps_hT[j][:, 0:D]).then_inc(hT_ready, 1)

            def move_diag(n):
                T, s = divmod(n, TG)
                dve.wait_ge(natural_landed[s], QN * DMA * (T + 1))
                if T >= 1:
                    dve.wait_ge(lo_ready, left_groups(T) - TG + s + 1)
                    dve.wait_ge(lo_ready2, left_groups(T) - TG + s + 1)
                nc.vector.transpose(diag[s][:, :, :].rearrange("p t (q r) -> p q t r", q=QN),
                                    natural[s][:, :, T * GW:(T + 1) * GW].rearrange("p q (t c) -> p q t c", c=R)
                                    ).then_inc(diag_moved, 1)

            dve.wait_ge(x_landed[0], QN * DMA)
            moments(0)
            moments(1)
            dve.wait_ge(x_landed[1], QN * DMA)
            moments(2)
            dve.wait_ge(mean_ready, 1)
            centre(0)
            centre(1)
            moments(3)
            move_hT(0)
            for c in range(1, XP):
                dve.wait_ge(mean_ready, c + 1)
                if c + 1 < XP:
                    dve.wait_ge(x_landed[c + 1], QN * DMA)
                with dve.Fori(c * XT // AR, (c + 1) * XT // AR) as i:
                    centre(i)
                    if c + 1 < XP:
                        moments(i + XT // AR)
                    move_hT(i - 1)
                if c == 1:
                    move_diag(0)
                    move_diag(1)
            move_diag(2)
            move_hT(NT // AR - 1)
            move_diag(3)

            def subtract(k, src=at):
                slot = k % RING
                dve.wait_ge(hi_ready, k + 1)
                at_least(dve, group_used, k - RING + 1)
                nc.vector.tensor_tensor(out=lo[slot][:, 0:SPLIT, :], in0=src[slot][:, 0:SPLIT, :],
                                        in1=hi[slot][:, 0:SPLIT, :].bitcast(F32),
                                        op=ALU.subtract).then_inc(lo_ready, 1)

            def move(k, i, src):
                at_least(dve, lo_ready, at_free(k, i))
                at_least(dve, lo_ready2, at_free(k, i))
                nc.vector.transpose(at[k % RING][:, :, :].rearrange("p t (q r) -> p q t r", q=QN),
                                    src.rearrange("p q (t c) -> p q t c", c=R)).then_inc(at_ready, 1)

            def row_sums(n):
                dve.wait_ge(sum_made, n + 1)
                at_least(dve, sum_ready, n)
                nc.vector.tensor_tensor_reduce(
                    out=own_part[:, :], in0=ps_sum[n if n < TG else n % 2][:, 0:QN], in1=own_q[:, :], scale=1.0,
                    scalar=0.0, op0=ALU.mult, op1=ALU.add,
                    accum_out=row_sum[:, :]).then_inc(own_summed, 1)
                dve.wait_ge(own_summed, n + 1)
                at_least(dve, d_ready, n - 1)
                nc.vector.tensor_scalar(row_safe[n % 2][:, :], row_sum[:, :], TINY, None, ALU.max)
                nc.vector.tensor_scalar(row_pos[n % 2][:, :], row_sum[:, :], 0.0, None,
                                        ALU.is_gt).then_inc(sum_ready, 1)

            dve.wait_ge(consts_made, 1)
            dve.wait_ge(last_summed, QA * WHOLE)

            def sum_last(n):
                T, s = divmod(n, TG)
                dve.wait_ge(natural_landed[s], QN * DMA * (T + 1))
                nc.vector.tensor_reduce(out=part_sum[:, n, QA:QN], in_=natural[s][:, QA, :], op=ALU.add,
                                        axis=AX.X).then_inc(last_summed, QA)

            def make_G(n):
                if n < TG:
                    dve.wait_ge(hw_ready, n + 1)
                dve.wait_ge(d_ready, n + 1)
                nc.vector.tensor_scalar(G[:, n, 0, :], acc[:, n, :], d[:, n:n + 1], None,
                                        ALU.mult).then_inc(G_hi_made, 1)
                dve.wait_ge(G_hi_made, n + 1)
                nc.vector.scalar_tensor_tensor(
                    out=G[:, n, 1, :], in0=acc[:, n, :], scalar=d[:, n:n + 1],
                    in1=G[:, n, 0, :].bitcast(F32), op0=ALU.mult, op1=ALU.subtract).then_inc(G_ready, 1)

            for n in range(TG):
                if n >= WHOLE:
                    sum_last(n)
                row_sums(n)
                if n > 0:
                    make_G(n - 1)
            make_G(TG - 1)
            dve.wait_ge(hw_ready, NT)
            k = 0
            for n in range(TG - 1, NT):
                T, s = divmod(n, TG)
                if T >= 1:
                    for g in range(T):
                        move(k, s * T + g, natural[s][:, :, g * GW:(g + 1) * GW])
                        if g == 0:
                            dve.wait_ge(hi_saved, n - TG + 1)
                            nc.vector.tensor_tensor(out=acc[:, n - TG, :], in0=acc[:, n - TG, :],
                                                    in1=bank[:, s, D:2 * D], op=ALU.add).then_inc(acc_saved, 1)
                        if g > 0:
                            subtract(k - 1)
                        k += 1
                        if g == min(D_AT, T - 1):
                            row_sums(n)
                    if T < BUSY or s == TG - 1:
                        subtract(k - 1)
                if n + 1 < NT and (s < TG - 1 or T >= BUSY):
                    sum_last(n + 1)
                if T >= BUSY and s < TG - 1:
                    subtract(k - 1)
                if s < TG - 1:
                    move_diag(n + 1)
                if T >= 1:
                    make_G(n)
                if s == TG - 1:
                    for j in range(TG):
                        subtract(k, diag)
                        k += 1
                    if n + 1 < NT:
                        if T < BUSY:
                            sum_last(n + 1)
                        move_diag(n + 1)

            def finish(k):
                t, s = place(k), k % TG
                dve.wait_ge(group_used, group_end(k))
                if k < TG:
                    nc.vector.tensor_copy(hi_total, bank[:, s, 0:D]).then_inc(hi_totalled, 1)
                else:
                    nc.vector.tensor_tensor(out=hi_total, in0=bank[:, s, 0:D], in1=acc[:, t, :],
                                            op=ALU.add).then_inc(hi_totalled, 1)
                dve.wait_ge(hi_totalled, k + 1)
                nc.vector.tensor_tensor(out=total, in0=bank[:, s, D:2 * D], in1=hi_total,
                                        op=ALU.add).then_inc(bank_taken, 1)
                dve.wait_ge(bank_taken, k + 1)
                at_least(dve, stored[s], QN * DMA * (k // TG))
                nc.vector.scalar_tensor_tensor(out=result[s][:, :], in0=total, scalar=d[:, t:t + 1],
                                               in1=b_sb[:, :], op0=ALU.mult, op1=ALU.add).then_inc(biased_ready, 1)
                dve.wait_ge(biased_ready, k + 1)
                dve.wait_ge(x_again_landed[s], QN * DMA * (k // TG + 1))
                nc.vector.scalar_tensor_tensor(out=result[s][:, :], in0=result[s][:, :], scalar=0.0,
                                               in1=x_again[:, s, :], op0=ALU.max, op1=ALU.add).then_inc(result_ready, 1)

            dve.wait_ge(acc_saved, NT - TG)
            dve.wait_ge(b_landed, DMA)
            for u in range(PAIRS):
                slot = u % TG
                dve.wait_ge(natural_landed[slot], QN * DMA * (NT // TG + 2 * (u // TG + 1)))
                first = 0
                for T, s in pair(u):
                    W = NS - 1 - T
                    for g in range(W):
                        move(k, k - left_groups(NS), right_part(slot, first, W)[:, :, g * GW:(g + 1) * GW])
                        if k > left_groups(NS):
                            subtract(k - 1)
                        k += 1
                        for f in range(finished(k - 1), finished(k)):
                            finish(f)
                    first += W
            subtract(k - 1)
            for f in range(finished(k), NT):
                finish(f)

        @block.tensor
        def _(pe):
            def transpose_rows(i):
                for j in range(AR):
                    t = AR * i + j
                    pe.wait_ge(centred_ready, t + 1)
                    at_least(pe, hT_ready, t - AR + 1)
                    for f in range(KD):
                        last = nc.tensor.transpose(ps_hT[j][:, f * P:(f + 1) * P], centred[j][:, f * P:(f + 1) * P],
                                                   ident[:, :])
                    last.then_inc(hT_made, 1)

            def project(i):
                for j in range(AR):
                    t = AR * i + j
                    pe.wait_ge(hT_ready, t + 1)
                    at_least(pe, hw_ready, t - AR + 1)
                    for f in range(KD):
                        last = nc.tensor.matmul(bank[:, j, 0:D], hT[j][:, f * P:(f + 1) * P], w_sb[:, f, :],
                                                start=(f == 0), stop=(f == KD - 1))
                    last.then_inc(hw_made, 1)

            pe.wait_ge(consts_made, 1)
            pe.wait_ge(w_landed, DMA)
            transpose_rows(0)
            transpose_rows(1)
            project(0)
            with pe.Fori(1, NT // AR - 1) as i:
                transpose_rows(i + 1)
                project(i)

            def add_up(n, slot):
                pe.wait_ge(quarter_summed, QA * (n + 1))
                pe.wait_ge(last_summed, QA * (n + 1))
                nc.tensor.matmul(ps_sum[slot][:, 0:QN], same_r[:, :], part_sum[:, n, :],
                                 start=True, stop=True).then_inc(sum_made, 1)

            pe.wait_ge(hT_ready, NT)
            for n in range(WHOLE):
                add_up(n, n)
            project(NT // AR - 1)
            for n in range(WHOLE, TG):
                add_up(n, n)

            def multiply(k, slot, s, g, first, last):
                pe.wait_ge(hi_ready, k + 1)
                for j in range(TG):
                    nc.tensor.matmul(bank[:, s, :], hi[slot][:, j, :],
                                     G[:, g * TG + j, :, :].rearrange("p a f -> p (a f)"),
                                     start=(first and j == 0), stop=False)
                pe.wait_ge(lo_ready, k + 1)
                for j in range(TG):
                    if j == SPLIT:
                        pe.wait_ge(lo_ready2, k + 1)
                    mm = nc.tensor.matmul(bank[:, s, D:2 * D], lo[slot][:, j, :], G[:, g * TG + j, 0, :],
                                          start=False, stop=(last and j == TG - 1))
                mm.then_inc(group_used, 1)

            pe.wait_ge(hw_ready, NT)
            for T in range(NS):
                for i, (s, j0) in enumerate(rows_of(pe, T) if T else ()):
                    n = TG * T + s
                    pe.wait_ge(own_summed, n - 1)
                    add_up(n, i % 2)
                    pe.wait_ge(acc_saved, n - TG + 1)
                    for g in range(T):
                        multiply(left_groups(T) + s * T + g, (j0 + g) % RING, s, g, g == 0, False)
                pe.wait_ge(G_ready, TG * (T + 1))
                for s in range(TG):
                    multiply(left_groups(T) + TG * T + s, s, s, T, T == 0, True)
            for u, static_u, e in looped_pairs(pe):
                j = 0
                for part, (T, _) in enumerate(pair(static_u)):
                    pe.wait_ge(bank_taken, 2 * u + part + 1)
                    for g in range(NS - 1 - T):
                        multiply(right_groups(u) + j, j % RING, 2 * e + part, T + 1 + g, g == 0, g == NS - 2 - T)
                        j += 1


INPUTS = ["x", "adj", "L0_gnn_W", "L0_gnn_b"]


def kernel(**inputs):
    import concourse.bacc as bacc
    from concourse.bass_utils import run_bass_kernel_spmd

    nc = bacc.Bacc("TRN2", target_bir_lowering=False, num_devices=1)
    arrays, args = {}, []
    for name in INPUTS:
        a = np.ascontiguousarray(inputs[name])
        arrays[f"in_{name}"] = a
        args.append(nc.dram_tensor(f"in_{name}", a.shape, mybir.dt.from_np(a.dtype), kind="ExternalInput").ap())
    out = nc.dram_tensor("out", arrays["in_x"].shape, F32, kind="ExternalOutput").ap()
    build(nc, *args, out)
    r = run_bass_kernel_spmd(nc, [arrays], core_ids=[0])
    return r.results[0]["out"]
```
